# Optimizing a Trainium2 kernel written in Bass

```python
import numpy as np
import jax
import jax.numpy as jnp

def _softmax(x, axis=-1):
    return jax.nn.softmax(x, axis=axis)

def _gelu(x):
    return jax.nn.gelu(x, approximate=True)

def _silu(x):
    return jax.nn.silu(x)

def _sigmoid(x):
    return jax.nn.sigmoid(x)

def _layernorm(x, axis=-1, eps=1e-05):
    m = jnp.mean(x, axis=axis, keepdims=True)
    v = jnp.var(x, axis=axis, keepdims=True)
    return (x - m) / jnp.sqrt(v + eps)

def _scatter_add(tgt, idx, src, axis=0):
    return tgt.at[idx].add(src)

def _segment_sum(src, seg, n):
    return jax.ops.segment_sum(src, seg, n)
kernel_name = 'mk_adj_resnorm_d4_adj_r2_b9308a'

def setup_inputs(seed: int=0):
    np.random.seed(seed)
    _w = jnp.asarray

    def _rec_inputs():
        import jax
        import jax.numpy as jnp
        _gk = jax.random.key(seed)
        x = -0.0005207 + 1.001 * jax.random.normal(jax.random.fold_in(_gk, 1), (3327, 128), jnp.float32)
        _a = jax.random.bernoulli(jax.random.fold_in(_gk, 2), 0.00240457, (3327, 3327))
        _a = jnp.logical_or(_a, jnp.eye(3327, dtype=bool))
        _af = _a.astype(jnp.float32)
        _af = _af * jax.random.uniform(jax.random.fold_in(_gk, 3), (3327, 3327), jnp.float32, 0.05, 1)
        adj = _af
        return (x, adj)
    x, adj = _rec_inputs()

    def _L0_gnn_setup():
        import jax, jax.numpy as jnp
        import numpy as np
        import math
        N = 4096
        FIN = 128
        FOUT = 128
        key = jax.random.key(seed)
        k1, k2, k3, k4 = jax.random.split(key, 4)
        x = jax.random.normal(k1, (N, FIN), dtype=jnp.float32)
        adj = jax.random.uniform(k2, (N, N), dtype=jnp.float32)
        stdv = 1.0 / math.sqrt(FOUT)
        W = jax.random.uniform(k3, (FIN, FOUT), minval=-stdv, maxval=stdv, dtype=jnp.float32)
        b = jax.random.uniform(k4, (FOUT,), minval=-stdv, maxval=stdv, dtype=jnp.float32)
        return {'input': x, 'adj': adj, 'W': W, 'b': b}
    _L0_gnn_all = _L0_gnn_setup()
    _L0_gnn_in = {k: v for k, v in _L0_gnn_all.items() if k in ('W', 'b')}
    del _L0_gnn_all

    def _L1_gnn_setup():
        import jax, jax.numpy as jnp
        import numpy as np
        N = 4096
        D = 128
        ALPHA = 0.2
        NEG_INF = -9000000000000000.0
        key = jax.random.key(seed)
        k1, k2, k3, k4, k5, k6 = jax.random.split(key, 6)
        inputs = jax.random.normal(k1, (N, D), dtype=jnp.float32)
        adj = (jax.random.uniform(k2, (N, N)) < 32.0 / N).astype(jnp.float32)
        adj = jnp.maximum(adj, jnp.eye(N, dtype=jnp.float32))
        cmt_weight = jax.random.uniform(k3, (N, 1), dtype=jnp.float32)
        W = jax.random.normal(k4, (D, D), dtype=jnp.float32) * (1.0 / np.sqrt(D))
        a1 = jax.random.normal(k5, (D, 1), dtype=jnp.float32) * 0.1
        a2 = jax.random.normal(k6, (D, 1), dtype=jnp.float32) * 0.1
        return {'inputs': inputs, 'adj': adj, 'cmt_weight': cmt_weight, 'W': W, 'a1': a1, 'a2': a2}
    _L1_gnn_all = _L1_gnn_setup()
    _L1_gnn_in = {k: v for k, v in _L1_gnn_all.items() if k in ('cmt_weight', 'W', 'a1', 'a2')}
    del _L1_gnn_all

    def _L2_gnn_setup():
        import jax, jax.numpy as jnp
        import numpy as np
        N = 4096
        IN_F = 128
        OUT_F = 128
        key = jax.random.key(seed)
        ks = jax.random.split(key, 7)
        feats = jax.random.normal(ks[0], (N, IN_F), dtype=jnp.float32)
        node_adj = jax.random.normal(ks[1], (N, N), dtype=jnp.float32)
        edge_adj = jax.random.normal(ks[2], (N, N), dtype=jnp.float32)
        node_weight = jax.random.normal(ks[3], (2 * IN_F, OUT_F), dtype=jnp.float32) * 0.05
        node_bias = jax.random.normal(ks[4], (OUT_F,), dtype=jnp.float32) * 0.05
        edge_weight = jax.random.normal(ks[5], (IN_F, OUT_F), dtype=jnp.float32) * 0.05
        edge_bias = jax.random.normal(ks[6], (OUT_F,), dtype=jnp.float32) * 0.05
        return {'feats': feats, 'node_adj': node_adj, 'edge_adj': edge_adj, 'node_weight': node_weight, 'node_bias': node_bias, 'edge_weight': edge_weight, 'edge_bias': edge_bias}
    _L2_gnn_all = _L2_gnn_setup()
    _L2_gnn_in = {k: v for k, v in _L2_gnn_all.items() if k in ('node_weight', 'node_bias', 'edge_weight', 'edge_bias')}
    del _L2_gnn_all

    def _L3_gnn_setup():
        import jax, jax.numpy as jnp
        import numpy as np
        N, H, HEADS = (2048, 128, 3)
        ALPHA = 0.2
        NEG_INF = -9000000000000000.0

        def _sign_adj(key, n, density):
            k1, k2 = jax.random.split(key)
            mask = jax.random.uniform(k1, (n, n)) < density
            sign = jnp.where(jax.random.uniform(k2, (n, n)) < 0.5, -1.0, 1.0)
            adj = jnp.where(mask, sign, 0.0).astype(jnp.float32)
            idx = jnp.arange(n)
            return adj.at[idx, idx].set(1.0)

        def _gru_cell(x, hstate, Wih, Whh, bih, bhh):
            gi = x @ Wih.T + bih
            gh = hstate @ Whh.T + bhh
            ir, iz, inn = jnp.split(gi, 3, axis=1)
            hr, hz, hn = jnp.split(gh, 3, axis=1)
            r = jax.nn.sigmoid(ir + hr)
            z = jax.nn.sigmoid(iz + hz)
            n = jnp.tanh(inn + r * hn)
            return (1.0 - z) * n + z * hstate

        def _gat_head(h, node_adj, edge_adj, W, a):
            hW = h @ W
            hp = (node_adj > 0).astype(hW.dtype) @ hW
            hm = (node_adj < 0).astype(hW.dtype) @ hW
            e_plus = jax.nn.leaky_relu(jnp.concatenate([hp, hm], axis=1) @ a, ALPHA)[:, 0]
            e_minus = jax.nn.leaky_relu(jnp.concatenate([hm, hp], axis=1) @ a, ALPHA)[:, 0]
            att = jnp.where(edge_adj > 0, e_plus[None, :], NEG_INF)
            att = jnp.where(edge_adj < 0, e_minus[None, :], att)
            att = jax.nn.softmax(att, axis=1)
            return att * edge_adj @ hW
        key = jax.random.key(seed)
        ks = jax.random.split(key, 16)
        std = 0.01
        gain = 1.414
        return {'h': jax.random.normal(ks[0], (N, H), jnp.float32), 'node_adj': _sign_adj(ks[1], N, 0.005), 'edge_adj': _sign_adj(ks[2], N, 0.005), 'gat_W': jax.random.normal(ks[3], (HEADS, H, H), jnp.float32) * (gain / np.sqrt(H, dtype=np.float32)), 'gat_a': jax.random.normal(ks[4], (HEADS, 2 * H, 1), jnp.float32) * 0.1, 'edge_Wih': jax.random.normal(ks[5], (3 * H, H), jnp.float32) * std, 'edge_Whh': jax.random.normal(ks[6], (3 * H, H), jnp.float32) * std, 'edge_bih': jnp.zeros((3 * H,), jnp.float32), 'edge_bhh': jnp.zeros((3 * H,), jnp.float32), 'node_Wih': jax.random.normal(ks[7], (3 * H, H), jnp.float32) * std, 'node_Whh': jax.random.normal(ks[8], (3 * H, H), jnp.float32) * std, 'node_bih': jnp.zeros((3 * H,), jnp.float32), 'node_bhh': jnp.zeros((3 * H,), jnp.float32)}
    _L3_gnn_all = _L3_gnn_setup()
    _L3_gnn_in = {k: v for k, v in _L3_gnn_all.items() if k in ('gat_W', 'gat_a', 'edge_Wih', 'edge_Whh', 'edge_bih', 'edge_bhh', 'node_Wih', 'node_Whh', 'node_bih', 'node_bhh')}
    del _L3_gnn_all
    return {'x': x, 'adj': adj, 'L0_gnn_W': _L0_gnn_in['W'], 'L0_gnn_b': _L0_gnn_in['b'], 'L1_gnn_cmt_weight': _L1_gnn_in['cmt_weight'], 'L1_gnn_W': _L1_gnn_in['W'], 'L1_gnn_a1': _L1_gnn_in['a1'], 'L1_gnn_a2': _L1_gnn_in['a2'], 'L2_gnn_node_weight': _L2_gnn_in['node_weight'], 'L2_gnn_node_bias': _L2_gnn_in['node_bias'], 'L2_gnn_edge_weight': _L2_gnn_in['edge_weight'], 'L2_gnn_edge_bias': _L2_gnn_in['edge_bias'], 'L3_gnn_gat_W': _L3_gnn_in['gat_W'], 'L3_gnn_gat_a': _L3_gnn_in['gat_a'], 'L3_gnn_edge_Wih': _L3_gnn_in['edge_Wih'], 'L3_gnn_edge_Whh': _L3_gnn_in['edge_Whh'], 'L3_gnn_edge_bih': _L3_gnn_in['edge_bih'], 'L3_gnn_edge_bhh': _L3_gnn_in['edge_bhh'], 'L3_gnn_node_Wih': _L3_gnn_in['node_Wih'], 'L3_gnn_node_Whh': _L3_gnn_in['node_Whh'], 'L3_gnn_node_bih': _L3_gnn_in['node_bih'], 'L3_gnn_node_bhh': _L3_gnn_in['node_bhh']}

def reference(x, adj, L0_gnn_W, L0_gnn_b, L1_gnn_cmt_weight, L1_gnn_W, L1_gnn_a1, L1_gnn_a2, L2_gnn_node_weight, L2_gnn_node_bias, L2_gnn_edge_weight, L2_gnn_edge_bias, L3_gnn_gat_W, L3_gnn_gat_a, L3_gnn_edge_Wih, L3_gnn_edge_Whh, L3_gnn_edge_bih, L3_gnn_edge_bhh, L3_gnn_node_Wih, L3_gnn_node_Whh, L3_gnn_node_bih, L3_gnn_node_bhh):
    import jax
    import jax.numpy as jnp

    def _L0_gnn_ref(input, adj, W, b):
        import jax, jax.numpy as jnp
        import numpy as np
        import math
        N = 4096
        FIN = 128
        FOUT = 128
        A = adj + jnp.eye(adj.shape[0], dtype=adj.dtype)
        D = 1.0 / jnp.sqrt(jnp.sum(A, axis=1))
        A = A * D[:, None] * D[None, :]
        support = input @ W
        out = A @ support
        return jax.nn.relu(out + b)

    def _L1_gnn_ref(inputs, adj, cmt_weight, W, a1, a2):
        import jax, jax.numpy as jnp
        import numpy as np
        N = 4096
        D = 128
        ALPHA = 0.2
        NEG_INF = -9000000000000000.0
        Wh = inputs @ W
        f1 = Wh @ a1
        f2 = Wh @ a2
        e = jax.nn.leaky_relu(f1 + f2.T, negative_slope=ALPHA)
        scores = jnp.where(adj > 0, e, NEG_INF)
        att = jax.nn.softmax(scores, axis=-1)
        node_out = jax.nn.relu(att @ Wh)
        return node_out

    def _L2_gnn_ref(feats, node_adj, edge_adj, node_weight, node_bias, edge_weight, edge_bias):
        import jax, jax.numpy as jnp
        import numpy as np
        N = 4096
        IN_F = 128
        OUT_F = 128
        pos = jnp.matmul((node_adj > 0).astype(feats.dtype), feats)
        neg = jnp.matmul((node_adj < 0).astype(feats.dtype), feats)
        node_support = jnp.concatenate([pos, neg], axis=1)
        node_output = jnp.matmul(node_support, node_weight)
        node_output = node_output + node_bias * jnp.diagonal(edge_adj)[:, None]
        edge_support = jnp.matmul(edge_adj, feats)
        edge_output = jnp.matmul(edge_support, edge_weight)
        edge_output = edge_output + edge_bias * jnp.diagonal(node_adj)[:, None]
        return node_output + edge_output

    def _L3_gnn_ref(h, node_adj, edge_adj, gat_W, gat_a, edge_Wih, edge_Whh, edge_bih, edge_bhh, node_Wih, node_Whh, node_bih, node_bhh):
        import jax, jax.numpy as jnp
        import numpy as np
        N, H, HEADS = (2048, 128, 3)
        ALPHA = 0.2
        NEG_INF = -9000000000000000.0

        def _sign_adj(key, n, density):
            k1, k2 = jax.random.split(key)
            mask = jax.random.uniform(k1, (n, n)) < density
            sign = jnp.where(jax.random.uniform(k2, (n, n)) < 0.5, -1.0, 1.0)
            adj = jnp.where(mask, sign, 0.0).astype(jnp.float32)
            idx = jnp.arange(n)
            return adj.at[idx, idx].set(1.0)

        def _gru_cell(x, hstate, Wih, Whh, bih, bhh):
            gi = x @ Wih.T + bih
            gh = hstate @ Whh.T + bhh
            ir, iz, inn = jnp.split(gi, 3, axis=1)
            hr, hz, hn = jnp.split(gh, 3, axis=1)
            r = jax.nn.sigmoid(ir + hr)
            z = jax.nn.sigmoid(iz + hz)
            n = jnp.tanh(inn + r * hn)
            return (1.0 - z) * n + z * hstate

        def _gat_head(h, node_adj, edge_adj, W, a):
            hW = h @ W
            hp = (node_adj > 0).astype(hW.dtype) @ hW
            hm = (node_adj < 0).astype(hW.dtype) @ hW
            e_plus = jax.nn.leaky_relu(jnp.concatenate([hp, hm], axis=1) @ a, ALPHA)[:, 0]
            e_minus = jax.nn.leaky_relu(jnp.concatenate([hm, hp], axis=1) @ a, ALPHA)[:, 0]
            att = jnp.where(edge_adj > 0, e_plus[None, :], NEG_INF)
            att = jnp.where(edge_adj < 0, e_minus[None, :], att)
            att = jax.nn.softmax(att, axis=1)
            return att * edge_adj @ hW
        dn = jnp.diag(node_adj)
        de = jnp.diag(edge_adj)
        idx = jnp.arange(node_adj.shape[0])
        node_adj_norm = node_adj.at[idx, idx].add(-dn)
        edge_adj_norm = edge_adj.at[idx, idx].add(-de)
        node_support = node_adj_norm @ h
        edge_output = _gru_cell(node_support, h, edge_Wih, edge_Whh, edge_bih, edge_bhh)
        edge_support = _gat_head(h, node_adj_norm, edge_adj_norm, gat_W[0], gat_a[0])
        for i in range(1, HEADS):
            edge_support = edge_support + _gat_head(h, node_adj_norm, edge_adj_norm, gat_W[i], gat_a[i])
        edge_support = edge_support / HEADS
        node_output = _gru_cell(edge_support, h, node_Wih, node_Whh, node_bih, node_bhh)
        return de[:, None] * edge_output + dn[:, None] * node_output
    x = _layernorm(x + _L0_gnn_ref(x, adj, L0_gnn_W, L0_gnn_b), axis=-1)
    x = _layernorm(x + _L1_gnn_ref(x, adj, L1_gnn_cmt_weight, L1_gnn_W, L1_gnn_a1, L1_gnn_a2), axis=-1)
    x = _layernorm(x + _L2_gnn_ref(x, adj, adj, L2_gnn_node_weight, L2_gnn_node_bias, L2_gnn_edge_weight, L2_gnn_edge_bias), axis=-1)
    x = _layernorm(x + _L3_gnn_ref(x, adj, adj, L3_gnn_gat_W, L3_gnn_gat_a, L3_gnn_edge_Wih, L3_gnn_edge_Whh, L3_gnn_edge_bih, L3_gnn_edge_bhh, L3_gnn_node_Wih, L3_gnn_node_Whh, L3_gnn_node_bih, L3_gnn_node_bhh), axis=-1)
    return x

_drawn_inputs = setup_inputs


def setup_inputs(seed=0):
    import zlib

    import numpy as np

    out = dict(_drawn_inputs(seed))
    spreads = {'L3_gnn_edge_bih': (0.0, 0.462),
     'L3_gnn_edge_bhh': (0.0, 0.695),
     'L3_gnn_node_bih': (0.0, 0.437),
     'L3_gnn_node_bhh': (0.0, 0.646)}
    factors = {'L2_gnn_node_bias': 4.273,
     'L2_gnn_edge_bias': 4.106,
     'L3_gnn_gat_W': 6.918,
     'L3_gnn_gat_a': 8.0,
     'L3_gnn_edge_Whh': 4.211,
     'L3_gnn_node_Wih': 6.749,
     'L3_gnn_node_Whh': 4.206}
    for name, (base, spread) in spreads.items():
        noise = np.random.default_rng([zlib.crc32(name.encode()), seed]).standard_normal(out[name].shape)
        drawn = base * np.exp(spread * noise) if base else spread * noise
        out[name] = jnp.asarray(drawn.astype(out[name].dtype))
    for name, factor in factors.items():
        out[name] = (out[name] * factor).astype(out[name].dtype)
    return out
```

```python
from contextlib import ExitStack

import concourse.bass as bass
from concourse import mybir
from concourse.alu_op_type import AluOpType as ALU

ACT = mybir.ActivationFunctionType
AX = mybir.AxisListType
F32, BF16, F16, I8, I32 = (mybir.dt.float32, mybir.dt.bfloat16, mybir.dt.float16, mybir.dt.int8, mybir.dt.int32)

N, F = 3327, 128
P = 128
TILES = -(-N // P)
NP = TILES * P
GROUPS = TILES // 2
PAIRS = GROUPS // 2
GW = 2 * P
CHUNKS = GROUPS
CW = 2 * GW
HEADS = 3
ALPHA = 0.2
EPS = 1e-5
NO_EDGE = -127.0
CODE = 2.0 ** 46
PAD_SCORE = -1e38
MAX_WIDTH = 512
BLOCKS = [(o, min(MAX_WIDTH, NP - o)) for o in range(0, NP, MAX_WIDTH)]
G3 = 3 * F
VR = 6 * HEADS


def program(nc, d, out):
    ctx = ExitStack()
    with ctx:
        def sb(name, shape, dt=F32):
            return ctx.enter_context(nc.sbuf_tensor(name, shape, dt))

        def sem(name):
            return ctx.enter_context(nc.semaphore(name))

        x = sb("x", [P, TILES, F])
        y = sb("y", [P, TILES, F])
        xT = sb("xT", [P, NP])
        es = sb("es", [P, TILES, F])
        ebc = sb("ebc", [P, NP])
        shared = sb("shared", [P, NP])
        x16 = shared[:].bitcast(F16).rearrange("p (t k f) -> p t k f", t=TILES, k=2)
        V = shared[0:VR, :]
        ring = sb("ring", [P, CHUNKS, CW])
        Pb = sb("Pb", [P, 2, 2, NP])
        code = sb("code", [P, 2, 2, NP], I8)
        work = code[:].rearrange("p a b n -> p (a b n)").bitcast(F32)
        qt = sb("qt", [P, 2, CW])
        mask = qt[:, :, 0:CW // 2].bitcast(F16)
        nmask = qt[:, :, CW // 2:CW].bitcast(F16)
        ub = sb("ub", [P, 2, GW])
        upb = work[:, 0:2 * GW].rearrange("p (a n) -> p a n", a=2)
        unb = work[:, 2 * GW:4 * GW].rearrange("p (a n) -> p a n", a=2)
        stage = sb("stage", [P, 2, GW])
        hstage = sb("hstage", [P, 2, GW])
        gstage = sb("gstage", [P, 2, 2, VR], BF16)
        nstage = sb("nstage", [P, 2, 2, VR], BF16)
        hb = sb("hb", [P, 2, F])
        ident = sb("ident", [P, P])
        identb = sb("identb", [P, P], BF16)
        nident = sb("nident", [P, P], I8)
        ones = sb("ones", [P, P])
        sel = sb("sel", [VR, 2 * HEADS, P])
        bd = es[:].bitcast(I8)[:, 0:TILES // 4 + 1].rearrange("p a f -> p (a f)")[:, 0:NP].rearrange("p (t c) -> p t c", c=P)
        wrep = sb("wrep", [P, P])
        W0 = sb("W0", [P, F])
        W1 = sb("W1", [P, F])
        W1T = sb("W1T", [P, F])
        a1 = sb("a1", [P, 2])
        w12 = sb("w12", [P, 2])
        W2 = sb("W2", [P, 3, F])
        gW = sb("gW", [P, HEADS, F])
        gWT = sb("gWT", [P, HEADS, F])
        wk = sb("wk", [P, F])
        selk = sb("selk", [VR, 2, P])
        epsc = sb("epsc", [P, 1])
        ga = sb("ga", [P, HEADS, 2])
        v6 = sb("v6", [P, 2, HEADS])
        gru = sb("gru", [P, 4, G3])
        gb = sb("gb", [P, 2, 4, F])
        gs = sb("gs", [P, TILES, VR + VR // 2], BF16)
        b0 = sb("b0", [P, F])
        b2 = sb("b2", [P, F])
        stats = sb("stats", [P, TILES, 6])
        cols = sb("cols", [P, 16, TILES])
        rs, sd, D, dg, mn, nf1, zs, std, rstd, ndg, npos, fin, mean, var, diff, nneg = (cols[:, k, :] for k in range(16))
        m2 = sb("m2", [P, 2, 2])
        um = sb("um", [P, 2, 2])
        nm = sb("nm", [P, 2, 2])
        rz = sb("rz", [P, 2, 2])
        row = sb("row", [1, 4])
        flag = sb("flag", [1, 4], I32)

        ps = ctx.enter_context(nc.psum_tensor("ps", [P, 8, MAX_WIDTH], F32))

        def UA(par):
            return ps[:, par, 0:GW]

        def U0(g):
            return ps[:].rearrange("p b n -> p (b n)")[:, bass.ds(g * GW, GW)]

        def Z0(par):
            return ps[:, (7, 0)[par], 0:GW].rearrange("p (a f) -> p a f", a=2)

        def UP(par):
            return ps[:, 2 + par, 0:GW]

        def UN(par):
            return ps[:, 4 + par, 0:GW]

        def Z(par):
            return ps[:, 6 + par, 0:GW].rearrange("p (a f) -> p a f", a=2)

        def TB(k):
            return ps[:, 2 + k, :]

        def GT(par):
            return ps[:, 4 + 2 * par:6 + 2 * par, :]

        xT_kept = nc.dram_tensor("xT_kept", [P, NP], F32, kind="Internal").ap()
        ncodes = nc.dram_tensor("ncodes", [GROUPS, P, 2, NP], I8, kind="Internal").ap()
        codes = nc.dram_tensor("codes", [GROUPS, P, 2, NP], I8, kind="Internal").ap()

        weights_in = sem("weights_in")
        consts = sem("consts")
        wprod = sem("wprod")
        wprod_out = sem("wprod_out")
        nat_in = [sem("nat_in0"), sem("nat_in1")]
        coded = sem("coded")
        code_out = [sem("code_out0"), sem("code_out1")]
        summed = sem("summed")
        diag_prod = sem("diag_prod")
        diag_done = sem("diag_done")
        diag_out = sem("diag_out")
        small = sem("small")
        flag_row = sem("flag_row")
        flag_ready = sem("flag_ready")
        ring_in = [sem(f"ring_in{c}") for c in range(CHUNKS)]
        ring_free = sem("ring_free")
        code_in = [sem("code_in0"), sem("code_in1")]
        root = sem("root")
        sd_done = sem("sd_done")
        D_done = sem("D_done")
        xs_done = sem("xs_done")
        staged = sem("staged")
        hstaged = sem("hstaged")
        mask_done = sem("mask_done")
        u_done = sem("u_done")
        u_out = sem("u_out")
        z_done = sem("z_done")
        z_out = sem("z_out")
        y_done = sem("y_done")
        st_done = sem("st_done")
        mv_done = sem("mv_done")
        x_done = sem("x_done")
        turned = sem("turned")
        xT_done = sem("xT_done")
        cols_done = sem("cols_done")
        e_done = sem("e_done")
        e_out = sem("e_out")
        wk_in = sem("wk_in")
        s_done = sem("s_done")
        shifted = sem("shifted")
        leaky = sem("leaky")
        e_leaky = sem("e_leaky")
        p_done = sem("p_done")
        t_done = sem("t_done")
        q_done = sem("q_done")
        q_done_s = sem("q_done_s")
        es_zero = sem("es_zero")
        mm_done = sem("mm_done")
        rz_done = sem("rz_done")
        pre_done = sem("pre_done")
        th_done = sem("th_done")
        gv = sem("gv")
        cand_done = sem("cand_done")
        n_done = sem("n_done")
        gru_done = sem("gru_done")
        un_out = sem("un_out")
        ncode_in = sem("ncode_in")
        ncoded = sem("ncoded")
        ncode_out = sem("ncode_out")
        spilled = sem("spilled")
        em_done = sem("em_done")
        em_out = sem("em_out")
        em_leaky = sem("em_leaky")
        nblock_in = [sem(f"nblock_in{b}") for b in range(4)]
        nstep = sem("nstep")
        xT_back = sem("xT_back")
        sync_passed = sem("sync_passed")
        vector_passed = sem("vector_passed")
        out_done = sem("out_done")
        block = ctx.enter_context(nc.Block())

        class Places:

            def __init__(self, order, buffers):
                self.order, self.buffers, self.lag = order, buffers, len(buffers) - 1
                assert len(order) == 2 * CHUNKS

            def at(self, par, c):
                return self.order[par * CHUNKS + c]

            def sbuf(self, par, c):
                return self.buffers[self.at(par, c)]

            def psum(self, par, c):
                return TB(self.at(par, c))

            def back(self, par, c):
                k = par * CHUNKS + c
                return next(n for n in range(1, 2 * CHUNKS) if self.order[k - n] == self.order[k])

            def earlier(self, base, g, par, c):
                back = self.back(par, c)
                if is_(g, 0) and back > c:
                    return base * CHUNKS
                return (base + g) * CHUNKS + c + 1 - back

        SCALAR_COPIES = (0, 3, 6, 9)
        VECTOR_COPIES = [c for c in range(CHUNKS) if c not in SCALAR_COPIES]

        def wait_copied(eng, unit, g, c):
            if isinstance(unit, int) and unit == 0:
                s, own = (q_done_s, SCALAR_COPIES) if c in SCALAR_COPIES else (q_done, VECTOR_COPIES)
                eng.wait_ge(s, g * len(own) + list(own).index(c) + 1)
            else:
                eng.wait_ge(q_done, GROUPS * len(VECTOR_COPIES) + ((unit - 1) * GROUPS + g) * CHUNKS + c + 1)

        def wait_bank(eng, unit, g, par, c, places):
            back = places.back(par, c)
            if c >= back:
                wait_copied(eng, unit, g, c - back)
            elif not is_(g, 0):
                wait_copied(eng, unit, g - 1, c - back + CHUNKS)
            elif not isinstance(unit, int):
                wait_copied(eng, unit, -1, CHUNKS - 1)

        flat = lambda a: a[:].rearrange("p a n -> p (a n)")
        four_places = Places([0, 1, 2, 3] * 3 + [0, 1, 2] + [0, 1, 2, 3] * 2 + [0, 1, 2],
                             [qt[:, 0], qt[:, 1], flat(stage), flat(hstage)])
        two_places = Places([0, 1] * CHUNKS, [qt[:, 0], qt[:, 1]])

        nblock = hstage[:].rearrange("p a n -> p (a n)").bitcast(I8).rearrange("p (q w) -> p q w", q=4)
        class Cells:

            def __init__(self, space):
                cells = space[:, 4 * F:16 * F].rearrange("p (k a f) -> p k a f", k=6, a=2)
                self.pre = space[:, 0:4 * F].rearrange("p (a f) -> p a f", a=2)
                self.hn, self.inn, self.rh, self.cand, self.n, self.hm = (cells[:, k] for k in range(6))

        one_space = Cells(work)
        two_spaces = [Cells(ring[:, 4 * par:4 * par + 4].rearrange("p c w -> p (c w)")) for par in range(2)]

        USES = ((GROUPS + 1) // 2, GROUPS // 2)
        CONSTS = 4 + 4 * HEADS
        W_ALL = 16 * 19
        NB = len(BLOCKS)
        NSTEPS = 1 + 2 * NB

        def groups(eng, body):
            body(0, 0, 0)
            body(1, 1, 0)
            with eng.Fori(0, (GROUPS - 3) // 2) as i:
                body(i * 2 + 2, 0, i + 1)
                body(i * 2 + 3, 1, i + 1)
            body(GROUPS - 1, 0, GROUPS // 2)

        def is_(g, k):
            return isinstance(g, int) and g == k

        def either(eng, section):
            eng.wait_ge(flag_ready, 1)
            negative = eng.value_load(flag[0:1, 0:1], min_val=0, max_val=1)
            with eng.If(negative):
                section(True)
            with eng.Else():
                section(False)

        def passed(eng, s):
            eng.sem_inc(s, 1)

        def ge(eng, s, value):
            if not isinstance(value, int) or value > 0:
                eng.wait_ge(s, value)

        @block.sync
        def _(sp):
            k = [(x[:], d["x"])]
            k += [(dst[:], d[name]) for dst, name in ((W0, "W0"), (W1, "W1"), (W1T, "W1T"), (a1, "a12"), (W2, "W2"),
                                                      (gW, "gW"), (gWT, "gWT"), (ga, "ga"), (gru, "gru"))]
            k += [(b0[:], d["b0"].to_broadcast([P, F])), (hb[:, 0], d["b2"][0:1].to_broadcast([P, F])),
                  (hb[:, 1], d["b2"][1:2].to_broadcast([P, F]))]
            for e in range(2):
                k += [(gb[:, e, 0:3].rearrange("p a f -> p (a f)"), d["gbi"][e:e + 1].to_broadcast([P, G3])),
                      (stage[:, e], d["gbh"][e:e + 1, 0:2 * F].to_broadcast([P, 2 * F])),
                      (gb[:, e, 3], d["gbh"][e:e + 1, 2 * F:].to_broadcast([P, F]))]
            assert 16 * len(k) == W_ALL
            for dst, src in k:
                sp.dma_start(dst, src).then_inc(weights_in, 16)

            def nat_load(g, par):
                sp.dma_start(Pb[:, par], d["adj"][g]).then_inc(nat_in[par], 16)

            def nat(g, par, n):
                if not is_(g, 0) and not is_(g, GROUPS - 1):
                    sp.wait_ge(diag_done, g)
                    passed(sp, sync_passed)
                    sp.wait_ge(summed, g * 2)
                    passed(sp, sync_passed)
                    nat_load(g + 1, 1 - par)
                for q in range(GROUPS):
                    sp.wait_ge(ring_free, g * GROUPS + q + 1)
                    passed(sp, sync_passed)
                    sp.dma_start(ring[:, q], d["adjT"][q, :, g]).then_inc(ring_in[q], 16)
                sp.wait_ge(coded, g + 1)
                passed(sp, sync_passed)
                sp.dma_start(codes[g], code[:, par]).then_inc(code_out[par], 16)

            sp.sem_inc(ring_free, CHUNKS)
            nat_load(0, 0)
            nat_load(1, 1)
            groups(sp, nat)

            def ring_group(pas, g, free, before):
                for c in range(CHUNKS):
                    sp.wait_ge(free, before + c + 1)
                    if c == 0 or pas == 3:
                        passed(sp, sync_passed)
                    sp.dma_start(ring[:, c], d["adjT"][g, :, c]).then_inc(ring_in[c], 16)

            def ring_pass(pas):
                with sp.Fori(0, GROUPS) as g:
                    ring_group(pas, g, ring_free, (g + pas * GROUPS) * CHUNKS)

            def code_load(unit, g, par):
                ge(sp, s_done, (unit * GROUPS + g) * 2 if is_(g, 0) else (unit * GROUPS + g - 1) * 2)
                passed(sp, sync_passed)
                sp.dma_start(code[:, par], codes[g]).then_inc(code_in[par], 16)

            sp.wait_ge(diag_done, GROUPS)
            for par in range(2):
                sp.wait_ge(code_out[par], 16 * USES[par])
            groups(sp, lambda g, par, n: code_load(0, g, par))
            ring_pass(1)
            for par in range(2):
                sp.wait_ge(code_in[par], 16 * USES[par])
            with sp.Fori(0, GROUPS) as g:
                for tt in range(2):
                    sp.dma_start(codes[bass.ds(g, 1), :, tt, bass.ds(g * GW + tt * P, P)].rearrange("o p c -> (o p) c"),
                                 bd[:, bass.ds(g * 2 + tt, 1), :].rearrange("p o c -> p (o c)")).then_inc(diag_out, 16)
            ring_pass(2)
            sp.wait_ge(diag_out, 16 * TILES)
            sp.wait_ge(gru_done, GROUPS)
            sp.wait_ge(ring_free, CHUNKS * (3 * GROUPS + 1))
            def heads(negative):
                if negative:
                    sp.sem_inc(ncode_out, 16)
                    with sp.Fori(0, GROUPS) as g:
                        sp.wait_ge(ncoded, g * 2 + 2)
                        passed(sp, sync_passed)
                        sp.dma_start(Pb[:, 0], d["adj"][bass.ds(g, 1)].rearrange("o p a n -> (o p) a n")).then_inc(ncode_in, 16)
                        sp.wait_ge(ncoded, g * 2 + 4)
                        passed(sp, sync_passed)
                        sp.dma_start(ncodes[bass.ds(g, 1)].rearrange("o p a n -> (o p) a n"), code[:, 0]).then_inc(ncode_out, 16)
                    sp.wait_ge(ncode_out, 16 * (GROUPS + 1))
                    sp.dma_start(xT_kept, xT[:]).then_inc(spilled, 16)
                    sp.wait_ge(spilled, 16)
                with sp.Fori(0, HEADS) as k:
                    def head_group(g, par, n):
                        if is_(g, 0):
                            code_load(k + 1, 0, 0)
                        if not is_(g, GROUPS - 1):
                            code_load(k + 1, g + 1, 1 - par)
                        if negative:
                            for tt in range(2):
                                for b, (o_, w) in enumerate(BLOCKS):
                                    t = (k * GROUPS + g) * 2 + tt
                                    if b >= 4:
                                        sp.wait_ge(nstep, t * NSTEPS + 2 * (b - 4) + 3)
                                    elif is_(g, 0) and tt == 0:
                                        sp.wait_ge(s_done, (k + 1) * TILES)
                                    else:
                                        sp.wait_ge(nstep, (t - 1) * NSTEPS + 2 * (b + NB - 4) + 3)
                                    passed(sp, sync_passed)
                                    sp.dma_start(nblock[:, (b + tt * NB) % 4, 0:w],
                                                 ncodes[bass.ds(g, 1), :, tt, o_:o_ + w].rearrange("o p w -> (o p) w")
                                                 ).then_inc(nblock_in[(b + tt * NB) % 4], 16)
                        ring_group(3, g, q_done, GROUPS * len(VECTOR_COPIES) + (k * GROUPS + g - 1) * CHUNKS)
                    groups(sp, head_group)
                if negative:
                    sp.wait_ge(s_done, (HEADS + 1) * TILES)
                    sp.dma_start(xT[:], xT_kept).then_inc(spilled, 16)
                    sp.wait_ge(spilled, 32)
                sp.sem_inc(xT_back, 1)
            either(sp, heads)
            full = N // P
            sp.wait_ge(x_done, 4 * TILES)
            sp.dma_start(out[0:full * P].rearrange("(t p) f -> p t f", p=P), x[:, 0:full]).then_inc(out_done, 16)
            sp.dma_start(out[full * P:N], x[0:N - full * P, full]).then_inc(out_done, 16)
            sp.wait_ge(out_done, 32)

        @block.gpsimd
        def _(pool):
            g_ = nc.gpsimd
            g_.memset(ones[:], 1.0).then_inc(consts, 1)
            pool.wait_ge(consts, 1)
            g_.affine_select(out=ident[:], in_=ones[:], compare_op=ALU.is_equal, fill=0.0, base=0,
                             pattern=[[-1, P]], channel_multiplier=1).then_inc(consts, 1)
            for k in range(2 * HEADS):
                g_.affine_select(out=sel[:, k], in_=ones[0:VR], compare_op=ALU.is_ge, fill=0.0, base=-3 * k,
                                 pattern=[[0, P]], channel_multiplier=1).then_inc(consts, 1)
            pool.wait_ge(consts, 2 + 2 * HEADS)
            for k in range(2 * HEADS):
                g_.affine_select(out=sel[:, k], in_=sel[:, k], compare_op=ALU.is_ge, fill=0.0, base=3 * k + 2,
                                 pattern=[[0, P]], channel_multiplier=-1).then_inc(consts, 1)
            g_.tensor_copy(identb[:], ident[:]).then_inc(consts, 1)
            g_.tensor_scalar(nident[:], ident[:], NO_EDGE, 0.0, ALU.mult, ALU.add).then_inc(consts, 1)

            pool.wait_ge(xT_done, 2 * NB)
            pool.wait_ge(small, GS_READY)

            def stage_l3(g, par, n):
                if not is_(g, 0):
                    pool.wait_ge(z_done, 2 + 3 * GROUPS + g - 1)
                g_.tensor_copy(hstage[:, par], xT[:, bass.ds(g * GW, GW)])
                g_.tensor_tensor(stage[:, par].rearrange("p (a f) -> p a f", a=2), x[:, bass.ds(g * 2, 2)],
                                 ndg[:, bass.ds(g * 2, 2), None].to_broadcast([P, 2, F]), ALU.mult)
                g_.tensor_tensor(gstage[:, par], gs[:, bass.ds(g * 2, 2), 0:VR],
                                 npos[:, bass.ds(g * 2, 2), None].to_broadcast([P, 2, VR]), ALU.mult)
                op = g_.tensor_tensor(nstage[:, par], gs[:, bass.ds(g * 2, 2), VR // 2:],
                                      nneg[:, bass.ds(g * 2, 2), None].to_broadcast([P, 2, VR]), ALU.mult)
                op.then_inc(staged, 1)
            groups(pool, stage_l3)

            pool.wait_ge(diag_out, 16 * TILES)
            g_.memset(es[:], 0.0).then_inc(es_zero, 1)
            with pool.Fori(0, HEADS) as k:
                pool.wait_ge(z_done, 2 + (k + 4) * GROUPS)
                g_.tensor_copy(wk[:], gW[:, bass.ds(k, 1)].rearrange("p o f -> p (o f)"))
                g_.tensor_copy(selk[:, 1], sel[:, bass.ds(k + HEADS, 1)].rearrange("p o f -> p (o f)"))
                g_.tensor_copy(selk[:, 0], sel[:, bass.ds(k, 1)].rearrange("p o f -> p (o f)")).then_inc(wk_in, 1)

            pool.wait_ge(z_out, 2 + 7 * GROUPS)
            pool.wait_ge(xT_back, 1)

            def stage_gru(g, par, n):
                if not is_(g, 0):
                    pool.wait_ge(u_done, 7 * GROUPS + g - 1)
                g_.tensor_copy(stage[:, par].rearrange("p (a f) -> p a f", a=2),
                               es[:, bass.ds(g * 2, 2)]).then_inc(staged, 1)
                if not is_(g, 0):
                    pool.wait_ge(z_done, 2 + 7 * GROUPS + g - 1)
                g_.tensor_copy(hstage[:, par], xT[:, bass.ds(g * GW, GW)]).then_inc(hstaged, 1)
            groups(pool, stage_gru)

        @block.scalar
        def _(act):
            A_ = nc.scalar.activation

            def copy_u(seq, g, par, scale=1.0, src=None):
                act.wait_ge(u_done, seq * GROUPS + g + 1)
                act.wait_ge(z_done, seq * GROUPS + g + (2 if is_(g, 0) else 1))
                return A_(ub[:, par], UA(par) if src is None else src, ACT.Copy, scale=scale)

            def roots(layer):
                act.wait_ge(mv_done, layer + 1)
                A_(std[:, :], var[:, :], ACT.Sqrt, bias=epsc[:], scale=1 / F).then_inc(root, 1)

            def turn_copies(first):
                for b, (o_, w) in enumerate(BLOCKS):
                    act.wait_ge(turned, first + b + 1)
                    A_(xT[:, o_:o_ + w], ps[:, b % 4, 0:w], ACT.Copy).then_inc(xT_done, 1)

            def score_copies(before):
                for b, (o_, w) in enumerate(BLOCKS):
                    act.wait_ge(e_done, before + b + 1)
                    A_(ebc[:, o_:o_ + w], ps[:, 4 + b % 2, 0:w], ACT.Copy, scale=1 / CODE).then_inc(e_out, 1)

            def sums(g, par, n):
                act.wait_ge(nat_in[par], (n + 1) * 16)
                for tt in range(2):
                    ge(act, summed, g * 2 + tt)
                    A_(ebc[:], Pb[:, par, tt], ACT.Copy, accum_out=rs[:, bass.ds(g * 2 + tt, 1)]).then_inc(summed, 1)
                act.wait_ge(summed, g * 2 + 2)
                A_(sd[:, bass.ds(g * 2, 2)], rs[:, bass.ds(g * 2, 2)], ACT.Sqrt, bias=ones[:, 0:1]).then_inc(sd_done, 1)
            act.wait_ge(consts, 1)
            groups(act, sums)
            groups(act, lambda g, par, n: copy_u(0, g, par, src=U0(g)).then_inc(u_out, 1))
            roots(0)
            turn_copies(0)
            score_copies(0)
            act.wait_ge(small, F1_READY)

            def copy_chunk1(g, par, c):
                act.wait_ge(t_done, g * CHUNKS + c + 1)
                ge(act, mm_done, four_places.earlier(0, g, par, c))
                A_(four_places.sbuf(par, c), four_places.psum(par, c), ACT.Copy).then_inc(q_done_s, 1)

            def shift(g, par, tt):
                t = g * 2 + tt
                act.wait_ge(s_done, t + 1)
                f = nf1[:, bass.ds(t, 1)]
                A_(um[:, par, tt:tt + 1], m2[:, par, tt:tt + 1], ACT.Identity, bias=f)
                A_(Pb[:, par, tt], Pb[:, par, tt], ACT.Identity, bias=f).then_inc(shifted, 1)

            def prob(g, par, tt):
                t = g * 2 + tt
                act.wait_ge(leaky, t + 1)
                A_(Pb[:, par, tt], Pb[:, par, tt], ACT.Exp, bias=nm[:, par, tt:tt + 1], scale=-1.0,
                   accum_out=zs[:, bass.ds(t, 1)]).then_inc(p_done, 1)

            def probs(g, par, n):
                if is_(g, 0):
                    shift(g, par, 0)
                    shift(g, par, 1)
                    prob(g, par, 0)
                    prob(g, par, 1)
                    return
                copy_chunk1(g - 1, 1 - par, SCALAR_COPIES[0])
                shift(g, par, 0)
                if not is_(g, 1):
                    copy_u(1, g - 2, par).then_inc(u_out, 1)
                copy_chunk1(g - 1, 1 - par, SCALAR_COPIES[1])
                shift(g, par, 1)
                copy_chunk1(g - 1, 1 - par, SCALAR_COPIES[2])
                prob(g, par, 0)
                copy_chunk1(g - 1, 1 - par, SCALAR_COPIES[3])
                prob(g, par, 1)
            groups(act, probs)
            copy_u(1, GROUPS - 2, 1).then_inc(u_out, 1)
            for c in SCALAR_COPIES:
                copy_chunk1(GROUPS - 1, 0, c)
            copy_u(1, GROUPS - 1, 0).then_inc(u_out, 1)
            roots(1)

            def copies2(g, par, n):
                copy_u(2, g, par)
                A_(upb[:, par], UP(par), ACT.Copy).then_inc(u_out, 1)
            groups(act, copies2)
            roots(2)

            turn_copies(NB)

            def gru_tanh(e, g, w):
                act.wait_ge(pre_done, e * GROUPS + g + 1)
                A_(w.pre, w.pre, ACT.Tanh, scale=0.5).then_inc(th_done, 1)

            def gru_cand(e, g, w):
                act.wait_ge(cand_done, e * GROUPS + g + 1)
                A_(w.n, w.cand, ACT.Tanh).then_inc(n_done, 1)

            def copies3(g, par, n):
                if not is_(g, 0):
                    gru_tanh(0, g - 1, one_space)
                    gru_cand(0, g - 1, one_space)
                copy_u(3, g, par)
                A_(V[:, bass.ds(g * GW, GW)], UP(par)[0:VR], ACT.Copy).then_inc(u_out, 1)
            groups(act, copies3)
            gru_tanh(0, GROUPS - 1, one_space)
            gru_cand(0, GROUPS - 1, one_space)

            with act.Fori(0, HEADS) as k:
                act.wait_ge(s_done, (k + 1) * TILES)
                score_copies((k + 1) * NB)

                def head_probs(g, par, n):
                    for tt in range(2):
                        act.wait_ge(s_done, (k + 1) * TILES + g * 2 + tt + 1)
                        A_(Pb[:, par, tt], Pb[:, par, tt], ACT.Exp, bias=m2[:, par, tt:tt + 1], scale=-1.0,
                           accum_out=zs[:, bass.ds(g * 2 + tt, 1)]).then_inc(p_done, 1)
                    if not is_(g, 0):
                        copy_u(k + 4, g - 1, 1 - par).then_inc(u_out, 1)
                groups(act, head_probs)
                copy_u(k + 4, GROUPS - 1, 0).then_inc(u_out, 1)

            def copies4(g, par, n):
                copy_u(7, g, par, scale=1.0 / HEADS).then_inc(u_out, 1)
                if not (is_(g, 0) or is_(g, 1)):
                    gru_cand(1, g - 2, two_spaces[par])
                if not is_(g, 0):
                    gru_tanh(1, g - 1, two_spaces[1 - par])
            groups(act, copies4)
            gru_cand(1, GROUPS - 2, two_spaces[1])
            gru_tanh(1, GROUPS - 1, two_spaces[0])
            gru_cand(1, GROUPS - 1, two_spaces[0])
            roots(3)

        @block.tensor
        def _(pe):
            mm = nc.tensor.matmul
            pe.sem_inc(z_done, 2)

            pe.wait_ge(weights_in, W_ALL)
            mm(ps[:, 7, 0:2], lhsT=W1T[:], rhs=a1[:], start=True, stop=True)
            for k in range(HEADS):
                last = mm(ps[:, 7, 2 + 2 * k:4 + 2 * k], lhsT=gWT[:, k], rhs=ga[:, k], start=True, stop=True)
            last.then_inc(wprod, 1)
            pe.wait_ge(consts, CONSTS)

            def product(seq, g, par, mats, Z=Z):
                pe.wait_ge(u_out, seq * GROUPS + g + 1)
                pe.wait_ge(z_out, seq * GROUPS + g + (2 if is_(g, 0) else 1))
                for tt in range(2):
                    for k, (u, w) in enumerate(mats(par)):
                        last = mm(Z(par)[:, tt], lhsT=u[:, tt * P:(tt + 1) * P], rhs=w, start=(k == 0),
                                  stop=(k == len(mats(par)) - 1))
                last.then_inc(z_done, 1)

            def u_finished(count):
                pe.wait_ge(ring_free, (count + 1) * CHUNKS)
                pe.sem_inc(u_done, 1)

            def turn(first, before):
                for b, (o_, w) in enumerate(BLOCKS):
                    pe.wait_ge(x_done, first + (o_ + w) // P)
                    if b >= 4:
                        pe.wait_ge(xT_done, before + b - 3)
                    for q in range(w // P):
                        last = nc.tensor.transpose(ps[:, b % 4, q * P:(q + 1) * P], x[:, o_ // P + q], ident[:])
                    last.then_inc(turned, 1)

            def scores(weight, src, before, ready=None):
                for b, (o_, w) in enumerate(BLOCKS):
                    if ready is not None:
                        pe.wait_ge(xT_done, ready + b + 1)
                    ge(pe, e_out, before + b - 1)
                    mm(ps[:, 4 + b % 2, 0:w], lhsT=weight, rhs=src[:, o_:o_ + w], start=True,
                       stop=True).then_inc(e_done, 1)

            def dense0(g, par, n):
                pe.wait_ge(xs_done, g + 1)
                for q in range(0, GROUPS, 2):
                    wide = min(2, GROUPS - q)
                    if q == GROUPS - 1:
                        for tt in range(2):
                            mm(U0(g)[:, tt * P:(tt + 1) * P], lhsT=stage[:, par, tt * P:(tt + 1) * P], rhs=ident[:],
                               start=False, stop=False)
                    for k in range(wide):
                        pe.wait_ge(ring_in[q + k], (g + 1) * 16)
                    for jj in range(2):
                        last = mm(ps[:, q // 2, 0:wide * GW].rearrange("p (a n) -> p a n", a=wide),
                                  lhsT=stage[:, par, jj * P:(jj + 1) * P], rhs=ring[:, q:q + wide, jj * GW:(jj + 1) * GW],
                                  start=(is_(g, 0) and jj == 0), stop=(is_(g, GROUPS - 1) and jj == 1))
                    last.then_inc(ring_free, wide)
            groups(pe, dense0)
            pe.wait_ge(ring_free, (GROUPS + 1) * CHUNKS)
            pe.sem_inc(u_done, GROUPS)
            pe.wait_ge(small, MIN_READY)
            mm(ps[0:1, 7, 2 * P:3 * P], lhsT=fin[:, 0:1], rhs=ident[:], start=True, stop=True).then_inc(flag_row, 1)
            pe.wait_ge(flag_ready, 1)
            groups(pe, lambda g, par, n: product(0, g, par, lambda q: [(ub[:, q], W0[:])], Z0))

            def attention(seq, unit, w, places):
                base = unit * GROUPS

                def turn_chunk(g, par, c):
                    k = (base + g) * CHUNKS + c
                    if c == 0:
                        pe.wait_ge(p_done, (base + g) * 2 + 2)
                    wait_bank(pe, unit, g, par, c, places)
                    for jj in range(2):
                        for tt in range(2):
                            last = nc.tensor.transpose(places.psum(par, c)[:, (2 * jj + tt) * P:(2 * jj + tt + 1) * P],
                                                       Pb[:, par, tt, (2 * c + jj) * P:(2 * c + jj + 1) * P], ident[:])
                    last.then_inc(t_done, 1)

                def use_chunk(g, par, c):
                    wait_copied(pe, unit, g, c)
                    for jj in range(2):
                        last = mm(UA(par), lhsT=x[:, 2 * c + jj], rhs=places.sbuf(par, c)[:, jj * GW:(jj + 1) * GW],
                                  start=(c == 0 and jj == 0), stop=(c == CHUNKS - 1 and jj == 1))
                    last.then_inc(mm_done, 1)
                    if c == CHUNKS - 1:
                        pe.wait_ge(mm_done, (base + g + 1) * CHUNKS)
                        pe.sem_inc(u_done, 1)

                def body(g, par, n):
                    for c in range(CHUNKS):
                        turn_chunk(g, par, c)
                        if c >= places.lag:
                            use_chunk(g, par, c - places.lag)
                        elif not is_(g, 0):
                            use_chunk(g - 1, 1 - par, CHUNKS - places.lag + c)
                        if c == 5 and not is_(g, 0):
                            product(seq, g - 1, 1 - par, lambda q: [(ub[:, q], w)])
                groups(pe, body)
                for c in range(CHUNKS - places.lag, CHUNKS):
                    use_chunk(GROUPS - 1, 0, c)
                product(seq, GROUPS - 1, 0, lambda q: [(ub[:, q], w)])

            turn(0, 0)
            pe.wait_ge(small, WREP_READY)
            scores(wrep[:], xT, 0, ready=0)
            for t in range(TILES):
                last = mm(ps[:, 6, t:t + 1], lhsT=xT[:, t * P:(t + 1) * P], rhs=w12[:, 0:1], start=True, stop=True)
            last.then_inc(cols_done, 1)
            attention(1, 0, W1[:], four_places)

            pe.wait_ge(x_done, 2 * TILES)
            pe.wait_ge(small, X16_READY)

            def layer2(negative):
                sums = lambda q: ([(ub[:, q], W2[:, 0]), (upb[:, q], W2[:, 1])] +
                                  ([(unb[:, q], W2[:, 2])] if negative else []))

                def product2(g, par):
                    if negative:
                        pe.wait_ge(un_out, g + 1)
                    product(2, g, par, sums)

                def dense2(g, par, n):
                    for c in range(CHUNKS):
                        pe.wait_ge(ring_in[c], (g + 1 + GROUPS) * 16)
                        pe.wait_ge(mask_done, g * CHUNKS + c + 1)
                        for jj in range(2):
                            cut = slice(jj * GW, (jj + 1) * GW)
                            first, final = (c == 0 and jj == 0), (c == CHUNKS - 1 and jj == 1)
                            for to, m in ((UP(par), mask), (UN(par), nmask))[:1 + negative]:
                                for k in range(2):
                                    mm(to, lhsT=x16[:, 2 * c + jj, k], rhs=m[:, (c + par) % 2, cut],
                                       start=first and k == 0, stop=final and k == 1)
                            last = mm(UA(par), lhsT=x[:, 2 * c + jj], rhs=ring[:, c, cut], start=first, stop=final)
                        last.then_inc(ring_free, 1)
                        if c == 1 and not is_(g, 0):
                            product2(g - 1, 1 - par)
                    u_finished(GROUPS + g + 1)
                groups(pe, dense2)
                product2(GROUPS - 1, 0)
            either(pe, layer2)

            turn(2 * TILES, NB)
            for t in range(TILES):
                if t % 4 == 0:
                    pe.wait_ge(xT_done, NB + t // 4 + 1)
                last = mm(ps[:, 6, 6 * t:6 * t + 6], lhsT=xT[:, t * P:(t + 1) * P],
                          rhs=v6[:].rearrange("p a k -> p (a k)"), start=True, stop=True)
            last.then_inc(cols_done, 1)
            pe.wait_ge(small, GS_READY)

            def gate_products(seq, e, g, par):
                pe.wait_ge(u_out, seq * GROUPS + g + 1)
                pe.wait_ge(z_out, seq * GROUPS + g + (2 if is_(g, 0) else 1))
                for tt in range(2):
                    cut = slice(tt * P, (tt + 1) * P)
                    gt = GT(par)[:, tt]
                    mm(gt[:, G3:4 * F], lhsT=hstage[:, par, cut], rhs=gru[:, 2 * e + 1, 2 * F:], start=True, stop=True)
                    mm(gt[:, 2 * F:G3], lhsT=ub[:, par, cut], rhs=gru[:, 2 * e, 2 * F:], start=True, stop=True)
                    mm(gt[:, 0:2 * F], lhsT=ub[:, par, cut], rhs=gru[:, 2 * e, 0:2 * F], start=True, stop=False)
                    last = mm(gt[:, 0:2 * F], lhsT=hstage[:, par, cut], rhs=gru[:, 2 * e + 1, 0:2 * F], start=False,
                              stop=True)
                last.then_inc(z_done, 1)

            def layer3(negative):
                masked = ((mask, 0, gstage), (nmask, VR // 2, nstage))[:1 + negative]

                def dense3(g, par, n):
                    for c in range(CHUNKS):
                        if c == CHUNKS - 1:
                            pe.wait_ge(staged, g + 1)
                            for tt in range(2):
                                cut = slice(tt * P, (tt + 1) * P)
                                for _, _, diagonal in masked:
                                    mm(UP(par)[0:VR, cut], lhsT=diagonal[:, par, tt], rhs=identb[:], start=False, stop=False)
                                mm(UA(par)[:, cut], lhsT=stage[:, par, cut], rhs=ident[:], start=False, stop=False)
                        pe.wait_ge(ring_in[c], (g + 1 + 2 * GROUPS) * 16)
                        pe.wait_ge(mask_done, (GROUPS + g) * CHUNKS + c + 1)
                        for jj in range(2):
                            cut = slice(jj * GW, (jj + 1) * GW)
                            first, final = (c == 0 and jj == 0), (c == CHUNKS - 1 and jj == 1)
                            for m, at, _ in masked:
                                mm(UP(par)[0:VR], lhsT=gs[:, 2 * c + jj, at:at + VR], rhs=m[:, (c + par) % 2, cut],
                                   start=first and at == 0, stop=final and m is masked[-1][0])
                            last = mm(UA(par), lhsT=x[:, 2 * c + jj], rhs=ring[:, c, cut], start=first, stop=final)
                        last.then_inc(ring_free, 1)
                        if c == 1 and not is_(g, 0):
                            gate_products(3, 0, g - 1, 1 - par)
                    u_finished(2 * GROUPS + g + 1)
                groups(pe, dense3)
            either(pe, layer3)
            gate_products(3, 0, GROUPS - 1, 0)

            pe.wait_ge(z_out, 2 + 4 * GROUPS)

            def heads(negative):
                with pe.Fori(0, HEADS) as k:
                    pe.wait_ge(wk_in, k + 1)
                    scores(selk[:, 0], V, (k + 1) * NB)
                    if negative:
                        pe.wait_ge(e_out, (k + 2) * NB)
                        for b, (o_, w) in enumerate(BLOCKS):
                            if b >= 2:
                                pe.wait_ge(em_out, k * NB + b - 1)
                            mm(ps[:, 4 + b % 2, 0:w], lhsT=selk[:, 1], rhs=V[:, o_:o_ + w], start=True,
                               stop=True).then_inc(em_done, 1)
                    attention(k + 4, k + 1, wk[:], two_places if negative else four_places)
            either(pe, heads)

            def node(g, par, n):
                pe.wait_ge(staged, GROUPS + g + 1)
                for tt in range(2):
                    cut = slice(tt * P, (tt + 1) * P)
                    last = nc.tensor.transpose(UA(par)[:, cut], stage[:, par, cut], ident[:])
                last.then_inc(u_done, 1)
                if not is_(g, 0):
                    pe.wait_ge(hstaged, g)
                    gate_products(7, 1, g - 1, 1 - par)
            pe.wait_ge(z_out, 2 + 7 * GROUPS)
            groups(pe, node)
            pe.wait_ge(hstaged, GROUPS)
            gate_products(7, 1, GROUPS - 1, 0)

        @block.vector
        def _(ve):
            v = nc.vector
            steps = [0]

            def step(ins):
                ins.then_inc(small, 1)
                steps[0] += 1
                ve.wait_ge(small, steps[0])

            ve.sem_inc(z_out, 2)
            step(v.memset(epsc[:], EPS))
            ve.wait_ge(weights_in, W_ALL)
            ve.wait_ge(consts, CONSTS)
            step(v.tensor_tensor(b2[:], hb[:, 0], hb[:, 1], ALU.add))
            step(v.tensor_tensor(gb[:, :, 0:2].rearrange("p e a f -> p e (a f)"),
                                 gb[:, :, 0:2].rearrange("p e a f -> p e (a f)"), stage[:], ALU.add))
            ve.wait_ge(wprod, 1)
            step(v.tensor_copy(w12[:], ps[:, 7, 0:2]))
            step(v.tensor_scalar(wrep[:], ones[:], w12[:, 1:2], None, ALU.mult))
            check(steps[0], WREP_READY)
            step(v.tensor_copy(v6[:], ps[:, 7, 2:2 + 2 * HEADS].rearrange("p (k a) -> p a k", a=2)))

            def tile(a, t):
                return a[:, bass.ds(t, 1)].rearrange("p o f -> p (o f)")

            def column(a, t):
                return a[:, bass.ds(t, 1)]

            def column2(a, g):
                return a[:, bass.ds(g * 2, 2)]

            def scan(g, par, n):
                ve.wait_ge(nat_in[par], (n + 1) * 16)
                ge(ve, diag_done, g)
                v.tensor_reduce(mn[:, bass.ds(g * 2, 2)], Pb[:, par], AX.X, ALU.min)
                ve.wait_ge(sd_done, g + 1)
                v.reciprocal(column2(D, g), column2(sd, g)).then_inc(D_done, 1)
                ve.wait_ge(D_done, g + 1)
                if not (is_(g, 0) or is_(g, 1)):
                    ve.wait_ge(ring_free, g * GROUPS)
                for tt in range(2):
                    op = v.tensor_scalar(stage[:, par, tt * P:(tt + 1) * P], tile(x, g * 2 + tt), column(D, g * 2 + tt),
                                         None, ALU.mult)
                op.then_inc(xs_done, 1)
                ge(ve, code_out[par], n * 16)
                v.tensor_scalar(code[:, par], Pb[:, par], 0.0, NO_EDGE, ALU.is_le, ALU.mult).then_inc(coded, 1)
                for tt in range(2):
                    op = v.tensor_tensor(hb[:, tt], Pb[:, par, tt, bass.ds(g * GW + tt * P, P)], ident[:], ALU.mult)
                op.then_inc(diag_prod, 1)
                ve.wait_ge(coded, g + 1)
                for tt in range(2):
                    v.tensor_tensor(bd[:, bass.ds(g * 2 + tt, 1)].rearrange("p o c -> p (o c)"),
                                    code[:, par, tt, bass.ds(g * GW + tt * P, P)], nident[:], ALU.min)
                ve.wait_ge(diag_prod, g + 1)
                v.tensor_reduce(dg[:, bass.ds(g * 2, 2)], hb[:], AX.X, ALU.add).then_inc(diag_done, 1)
            groups(ve, scan)
            ve.wait_ge(diag_done, GROUPS)
            step(v.tensor_reduce(fin[:, 0:1], mn[:, :], AX.X, ALU.min))
            check(steps[0], MIN_READY)
            step(v.tensor_scalar(ndg[:, :], dg[:, :], -1.0, None, ALU.mult))
            step(v.tensor_scalar(npos[:, :], dg[:, :], 0.0, -1.0, ALU.is_gt, ALU.mult))
            step(v.tensor_scalar(nneg[:, :], dg[:, :], 0.0, -1.0, ALU.is_lt, ALU.mult))
            ve.wait_ge(flag_row, 1)
            step(v.tensor_reduce(row[0:1, 0:1], ps[0:1, 7, 2 * P:3 * P], AX.X, ALU.min))
            v.tensor_scalar(flag[0:1, 0:1], row[0:1, 0:1], 0.0, None, ALU.is_lt).then_inc(flag_ready, 1)
            def statistics(layer, g):
                ve.wait_ge(y_done, layer * GROUPS + g + 1)
                passed(ve, vector_passed)
                for tt in range(2):
                    op = v.bn_stats(tile(stats, g * 2 + tt), tile(y, g * 2 + tt))
                op.then_inc(st_done, 1)

            def residual(seq, layer, g):
                ve.wait_ge(z_out, 2 + seq * GROUPS + g + 1)
                v.tensor_tensor(y[:, bass.ds(g * 2, 2)], hb[:], x[:, bass.ds(g * 2, 2)], ALU.add).then_inc(y_done, 1)
                statistics(layer, g)

            def norm(layer):
                ve.wait_ge(st_done, (layer + 1) * GROUPS)
                a, b = stats[:, :, 1], stats[:, :, 4]
                v.tensor_tensor(mean[:, :], a, b, ALU.add)
                v.tensor_tensor(var[:, :], stats[:, :, 2], stats[:, :, 5], ALU.add)
                step(v.tensor_tensor(diff[:, :], a, b, ALU.subtract))
                v.tensor_scalar(mean[:, :], mean[:, :], 0.5, None, ALU.mult)
                step(v.scalar_tensor_tensor(diff[:, :], diff[:, :], F / 4, diff[:, :], ALU.mult, ALU.mult))
                v.tensor_tensor(var[:, :], var[:, :], diff[:, :], ALU.add).then_inc(mv_done, 1)
                ve.wait_ge(root, layer + 1)
                step(v.reciprocal(rstd[:, :], std[:, :]))
                for t in range(TILES):
                    v.tensor_scalar(tile(x, t), tile(y, t), column(mean, t), column(rstd, t), ALU.subtract,
                                    ALU.mult).then_inc(x_done, 1)

            def finish0(g, par, n):
                ve.wait_ge(z_done, 2 + g + 1)
                for tt in range(2):
                    op = v.scalar_tensor_tensor(hb[:, tt], Z0(par)[:, tt], column(D, g * 2 + tt), b0[:], ALU.mult, ALU.add)
                op.then_inc(z_out, 1)
                ve.wait_ge(z_out, 2 + g + 1)
                v.scalar_tensor_tensor(y[:, bass.ds(g * 2, 2)], hb[:], 0.0, x[:, bass.ds(g * 2, 2)], ALU.max,
                                       ALU.add).then_inc(y_done, 1)
                statistics(0, g)
            groups(ve, finish0)
            norm(0)

            def attention(unit, times_A, finish, negative=False):
                base = unit * GROUPS
                places = two_places if negative else four_places
                own = range(CHUNKS) if times_A else VECTOR_COPIES

                def negative_scores(g, par, tt):
                    t = ((unit - 1) * GROUPS + g) * 2 + tt
                    for b, (o_, w) in enumerate(BLOCKS):
                        q = (b + tt * NB) % 4
                        uses = [(i + j * NB) % 4 for j in range(2) for i in range(NB)]
                        before = uses[:b + tt * NB].count(q)
                        ve.wait_ge(nblock_in[q], (((unit - 1) * GROUPS + g) * uses.count(q) + before + 1) * 16)
                        tmp = stage[:].rearrange("p a n -> p (a n)")[:, 0:w]
                        v.scalar_tensor_tensor(tmp, nblock[:, q, 0:w], -CODE, xT[:, o_:o_ + w], ALU.mult,
                                               ALU.subtract).then_inc(nstep, 1)
                        ve.wait_ge(nstep, t * NSTEPS + 2 * b + 2)
                        v.tensor_tensor(Pb[:, par, tt, o_:o_ + w], Pb[:, par, tt, o_:o_ + w], tmp, ALU.min).then_inc(nstep, 1)
                        ve.wait_ge(nstep, t * NSTEPS + 2 * b + 3)
                    v.tensor_reduce(m2[:, par, tt:tt + 1], Pb[:, par, tt], AX.X, ALU.min).then_inc(s_done, 1)

                def score(g, par, n, tt):
                    t = (base + g) * 2 + tt
                    if tt == 0:
                        ve.wait_ge(code_in[par], (unit * USES[par] + n + 1) * 16)
                    if is_(g, 0) and tt == 0 and times_A:
                        ve.wait_ge(e_leaky, unit * NB)
                    passed(ve, vector_passed)
                    v.tensor_tensor_reduce(Pb[:, par, tt], code[:, par, tt], ebc[:], -CODE, 3e38, ALU.add, ALU.min,
                                           m2[:, par, tt:tt + 1]).then_inc(nstep if negative else s_done, 1)
                    if negative:
                        ve.wait_ge(nstep, ((unit - 1) * TILES + g * 2 + tt) * NSTEPS + 1)
                        negative_scores(g, par, tt)

                def leaky_relu(g, par, tt):
                    t = g * 2 + tt
                    ve.wait_ge(shifted, t + 1)
                    v.scalar_tensor_tensor(nm[:, par, tt:tt + 1], um[:, par, tt:tt + 1], ALPHA, um[:, par, tt:tt + 1],
                                           ALU.mult, ALU.min)
                    v.scalar_tensor_tensor(Pb[:, par, tt], Pb[:, par, tt], ALPHA, Pb[:, par, tt], ALU.mult,
                                           ALU.min).then_inc(leaky, 1)

                def copy_chunk(g, par, c):
                    k = (base + g) * CHUNKS + c
                    ve.wait_ge(t_done, k + 1)
                    ge(ve, mm_done, places.earlier(base, g, par, c))
                    dst, src = places.sbuf(par, c), places.psum(par, c)
                    if times_A:
                        ve.wait_ge(ring_in[c], ((unit - 1) * GROUPS + g + 1 + 3 * GROUPS) * 16)
                        op = v.tensor_tensor(dst, src, ring[:, c], ALU.mult)
                    else:
                        op = v.tensor_copy(dst, src)
                    op.then_inc(q_done, 1)

                def body(g, par, n):
                    score(g, par, n, 0)
                    if is_(g, 0):
                        score(g, par, n, 1)
                        if not times_A:
                            leaky_relu(g, par, 0)
                            leaky_relu(g, par, 1)
                        return
                    for c in own:
                        copy_chunk(g - 1, 1 - par, c)
                        if c == 2:
                            score(g, par, n, 1)
                        if c == 5 and not times_A:
                            leaky_relu(g, par, 0)
                        if c == 8 and not times_A:
                            leaky_relu(g, par, 1)
                        if c == 10 and not is_(g, 1):
                            finish(g - 2, par)
                groups(ve, body)
                for c in own:
                    copy_chunk(GROUPS - 1, 0, c)
                    if c == 8:
                        finish(GROUPS - 2, 1)
                finish(GROUPS - 1, 0)

            ve.wait_ge(cols_done, 1)
            step(v.tensor_scalar(nf1[:, :], ps[:, 6, 0:TILES], -1.0, None, ALU.mult))
            check(steps[0], F1_READY)
            ve.wait_ge(e_out, NB)
            step(v.memset(ebc[:, N:NP], PAD_SCORE / CODE))

            def finish1(g, par):
                ve.wait_ge(z_done, 2 + GROUPS + g + 1)
                ge(ve, rz_done, g)
                v.reciprocal(rz[:, par], zs[:, bass.ds(g * 2, 2)]).then_inc(rz_done, 1)
                ve.wait_ge(rz_done, g + 1)
                for tt in range(2):
                    op = v.tensor_scalar(hb[:, tt], Z(par)[:, tt], rz[:, par, tt:tt + 1], 0.0, ALU.mult, ALU.max)
                op.then_inc(z_out, 1)
                residual(1, 1, g)
            attention(0, False, finish1)
            norm(1)

            ve.wait_ge(x_done, 2 * TILES)
            step(v.tensor_copy(x16[:, :, 0], x[:]))
            step(v.tensor_tensor(x16[:, :, 1], x[:], x16[:, :, 0], ALU.subtract))
            check(steps[0], X16_READY)

            def masks(pas, g, par, c, negative):
                k = (pas * GROUPS + g) * CHUNKS + c
                ve.wait_ge(ring_in[c], (g + 1 + pas * GROUPS) * 16)
                ve.wait_ge(ring_free, k + CHUNKS - 1)
                if negative:
                    v.tensor_scalar(nmask[:, (c + par) % 2], ring[:, c], 0.0, None, ALU.is_lt)
                v.tensor_scalar(mask[:, (c + par) % 2], ring[:, c], 0.0, None, ALU.is_gt).then_inc(mask_done, 1)

            def finish2(g, par):
                ve.wait_ge(z_done, 2 + 2 * GROUPS + g + 1)
                for tt in range(2):
                    op = v.scalar_tensor_tensor(hb[:, tt], b2[:], column(dg, g * 2 + tt), Z(par)[:, tt], ALU.mult, ALU.add)
                op.then_inc(z_out, 1)
                residual(2, 2, g)

            def layer2(negative):
                def copy_un(g, par):
                    if negative:
                        ve.wait_ge(u_done, 2 * GROUPS + g + 1)
                        v.tensor_copy(unb[:, par], UN(par)).then_inc(un_out, 1)

                def body2(g, par, n):
                    for c in range(CHUNKS):
                        masks(1, g, par, c, negative)
                        if c == 0 and not is_(g, 0):
                            copy_un(g - 1, 1 - par)
                        if c == 6 and not is_(g, 0):
                            finish2(g - 1, 1 - par)
                groups(ve, body2)
                copy_un(GROUPS - 1, 0)
            either(ve, layer2)
            finish2(GROUPS - 1, 0)
            norm(2)

            ve.wait_ge(cols_done, 2)
            g6 = ps[:, 6, 0:6 * TILES].rearrange("p (t r) -> p t r", r=6)
            part = [gs[:, :, 0:VR].rearrange("p t (r k) -> p t r k", k=3)[:, :, :, k] for k in range(3)]
            rest = ub[:].rearrange("p a n -> p (a n)")[:, 0:6 * TILES].rearrange("p (t r) -> p t r", r=6)
            step(v.tensor_copy(part[0], g6))
            step(v.tensor_tensor(rest, g6, part[0], ALU.subtract))
            step(v.tensor_copy(part[1], rest))
            step(v.tensor_tensor(rest, rest, part[1], ALU.subtract))
            step(v.tensor_copy(part[2], rest))
            step(v.tensor_copy(gs[:, :, VR:], gs[:, :, 0:VR // 2]))
            check(steps[0], GS_READY)

            def gru_a(seq, e, g, par, w, before):
                ve.wait_ge(z_done, 2 + seq * GROUPS + g + 1)
                ge(ve, gru_done, before)
                bias = gb[:, e].rearrange("p a f -> p (a f)")
                gt = GT(par)

                def b_(lo, hi):
                    return bias[:, None, lo:hi].to_broadcast([P, 2, hi - lo])
                v.tensor_tensor(w.pre, gt[:, :, 0:2 * F], b_(0, 2 * F), ALU.add).then_inc(pre_done, 1)
                v.tensor_tensor(w.hn, gt[:, :, G3:4 * F], b_(G3, 4 * F), ALU.add)
                v.tensor_tensor(w.inn, gt[:, :, 2 * F:G3], b_(2 * F, G3), ALU.add).then_inc(z_out, 1)

            def gru_b(seq, e, g, w):
                k = e * GROUPS + g
                ve.wait_ge(th_done, k + 1)
                ve.wait_ge(z_out, 2 + seq * GROUPS + g + 1)
                v.scalar_tensor_tensor(w.rh, w.pre[:, :, 0:F], 1.0, w.hn, ALU.add, ALU.mult).then_inc(gv, 1)
                ve.wait_ge(gv, k * 4 + 1)
                v.scalar_tensor_tensor(w.cand, w.rh, 0.5, w.inn, ALU.mult, ALU.add).then_inc(cand_done, 1)

            def gru_c(e, g, w, base):
                k = e * GROUPS + g
                ve.wait_ge(n_done, k + 1)
                v.tensor_tensor(w.hm, x[:, bass.ds(g * 2, 2)], w.n, ALU.subtract).then_inc(gv, 1)
                ve.wait_ge(gv, k * 4 + 2)
                v.scalar_tensor_tensor(w.rh, w.pre[:, :, F:2 * F], 1.0, w.hm, ALU.add, ALU.mult).then_inc(gv, 1)
                ve.wait_ge(gv, k * 4 + 3)
                v.scalar_tensor_tensor(w.hn, w.rh, 0.5, w.n, ALU.mult, ALU.add).then_inc(gv, 1)
                ve.wait_ge(gv, k * 4 + 4)
                for tt in range(2):
                    op = v.scalar_tensor_tensor(tile(y, g * 2 + tt), w.hn[:, tt], column(dg, g * 2 + tt),
                                                tile(base, g * 2 + tt), ALU.mult, ALU.add)
                op.then_inc(gru_done, 1)

            def layer3(negative):
                def body3(g, par, n):
                    for c in range(CHUNKS):
                        masks(2, g, par, c, negative)
                        if not is_(g, 0):
                            if c == 4:
                                gru_a(3, 0, g - 1, 1 - par, one_space, g - 1)
                            if c == 7:
                                gru_b(3, 0, g - 1, one_space)
                            if c == 10:
                                gru_c(0, g - 1, one_space, x)
                groups(ve, body3)
            either(ve, layer3)
            gru_a(3, 0, GROUPS - 1, 0, one_space, GROUPS - 1)
            gru_b(3, 0, GROUPS - 1, one_space)
            gru_c(0, GROUPS - 1, one_space, x)

            ve.wait_ge(es_zero, 1)
            def heads(negative):
                if negative:
                    ve.sem_inc(ncoded, 2)
                    with ve.Fori(0, GROUPS) as g:
                        ve.wait_ge(ncode_in, (g + 1) * 16)
                        ve.wait_ge(ncode_out, g * 16 + 16)
                        v.tensor_scalar(code[:, 0], Pb[:, 0], 0.0, NO_EDGE, ALU.is_ge, ALU.mult).then_inc(ncoded, 1)
                        ve.wait_ge(ncoded, g * 2 + 3)
                        for tt in range(2):
                            cut = code[:, 0, tt, bass.ds(g * GW + tt * P, P)]
                            op = v.tensor_tensor(cut, cut, nident[:], ALU.min)
                        op.then_inc(ncoded, 1)
                    ve.wait_ge(spilled, 16)
                with ve.Fori(0, HEADS) as k:
                    for b, (o_, w) in enumerate(BLOCKS):
                        ve.wait_ge(e_out, (k + 1) * NB + b + 1)
                        v.scalar_tensor_tensor(ebc[:, o_:o_ + w], ebc[:, o_:o_ + w], ALPHA, ebc[:, o_:o_ + w], ALU.mult,
                                               ALU.max).then_inc(e_leaky, 1)
                    if negative:
                        for b, (o_, w) in enumerate(BLOCKS):
                            ve.wait_ge(em_done, k * NB + b + 1)
                            v.tensor_copy(xT[:, o_:o_ + w], ps[:, 4 + b % 2, 0:w]).then_inc(em_out, 1)
                            ve.wait_ge(em_out, k * NB + b + 1)
                            v.scalar_tensor_tensor(xT[:, o_:o_ + w], xT[:, o_:o_ + w], ALPHA, xT[:, o_:o_ + w], ALU.mult,
                                                   ALU.max).then_inc(em_leaky, 1)
                        ve.wait_ge(em_leaky, (k + 1) * NB)
                    ve.wait_ge(z_out, 2 + (k + 4) * GROUPS)

                    def finish_head(g, par):
                        ve.wait_ge(z_done, 2 + (k + 4) * GROUPS + g + 1)
                        ve.wait_ge(rz_done, (k + 1) * GROUPS + g)
                        v.reciprocal(rz[:, par], zs[:, bass.ds(g * 2, 2)]).then_inc(rz_done, 1)
                        ve.wait_ge(rz_done, (k + 1) * GROUPS + g + 1)
                        for tt in range(2):
                            op = v.scalar_tensor_tensor(tile(es, g * 2 + tt), Z(par)[:, tt], rz[:, par, tt:tt + 1],
                                                        tile(es, g * 2 + tt), ALU.mult, ALU.add)
                        op.then_inc(z_out, 1)
                    attention(k + 1, True, finish_head, negative)
            either(ve, heads)

            def node_stats(g):
                ve.wait_ge(gru_done, GROUPS + g + 1)
                passed(ve, vector_passed)
                for tt in range(2):
                    op = v.bn_stats(tile(stats, g * 2 + tt), tile(y, g * 2 + tt))
                op.then_inc(st_done, 1)

            def body4(g, par, n):
                early = is_(g, 0) or is_(g, 1)
                if not early:
                    gru_c(1, g - 2, two_spaces[par], y)
                if not is_(g, 0):
                    gru_b(7, 1, g - 1, two_spaces[1 - par])
                if not early:
                    node_stats(g - 2)
                gru_a(7, 1, g, par, two_spaces[par], GROUPS if early else GROUPS + g - 1)
            groups(ve, body4)
            gru_c(1, GROUPS - 2, two_spaces[1], y)
            gru_b(7, 1, GROUPS - 1, two_spaces[0])
            node_stats(GROUPS - 2)
            gru_c(1, GROUPS - 1, two_spaces[0], y)
            node_stats(GROUPS - 1)
            norm(3)


def check(got, want):
    assert got == want, (got, want)


WREP_READY = 5
MIN_READY = 7
F1_READY = 15
X16_READY = 21
GS_READY = 30


def kernel(**inputs):
    import numpy as np
    from concourse import bacc
    from concourse.bass_utils import run_bass_kernel_spmd

    def get(name):
        return np.asarray(inputs[name])

    pad = NP - N
    adj = np.pad(get("adj"), ((0, pad), (0, pad)))
    xin = np.pad(get("x"), ((0, pad), (0, 0)))
    heads = get("L3_gnn_gat_W")
    arrays = {
        "adj": adj.reshape(GROUPS, 2, P, NP).transpose(0, 2, 1, 3),
        "adjT": adj.T.reshape(CHUNKS, 2, P, GROUPS, GW).transpose(3, 2, 0, 1, 4).reshape(GROUPS, P, CHUNKS, CW),
        "x": xin.reshape(TILES, P, F).transpose(1, 0, 2),
        "W0": get("L0_gnn_W"),
        "b0": get("L0_gnn_b")[None],
        "W1": get("L1_gnn_W"),
        "W1T": get("L1_gnn_W").T,
        "a12": np.concatenate([get("L1_gnn_a1"), get("L1_gnn_a2")], axis=1),
        "W2": np.stack([get("L2_gnn_edge_weight"), get("L2_gnn_node_weight")[:F], get("L2_gnn_node_weight")[F:]], axis=1),
        "b2": np.stack([get("L2_gnn_node_bias"), get("L2_gnn_edge_bias")]),
        "gW": heads.transpose(1, 0, 2),
        "gWT": heads.transpose(2, 0, 1),
        "ga": get("L3_gnn_gat_a").reshape(HEADS, 2, F).transpose(2, 0, 1),
        "gru": np.stack([get(f"L3_gnn_{n}").T for n in ("edge_Wih", "edge_Whh", "node_Wih", "node_Whh")], axis=1),
        "gbi": np.stack([get("L3_gnn_edge_bih"), get("L3_gnn_node_bih")]),
        "gbh": np.stack([get("L3_gnn_edge_bhh"), get("L3_gnn_node_bhh")]),
    }
    nc = bacc.Bacc("TRN2", target_bir_lowering=False, num_devices=1)
    arrays = {f"in_{k}": np.ascontiguousarray(a) for k, a in arrays.items()}
    d = {k[3:]: nc.dram_tensor(k, a.shape, mybir.dt.from_np(a.dtype), kind="ExternalInput").ap()
         for k, a in arrays.items()}
    out = nc.dram_tensor("out", (N, F), F32, kind="ExternalOutput").ap()
    program(nc, d, out)
    return run_bass_kernel_spmd(nc, [arrays], core_ids=[0]).results[0]["out"]
```
